# Optimizing a Trainium2 kernel written in Bass

```python
import numpy as np
import jax
import jax.numpy as jnp

def _softmax(x, axis=-1):
    return jax.nn.softmax(x, axis=axis)

def _gelu(x):
    return jax.nn.gelu(x, approximate=True)

def _silu(x):
    return jax.nn.silu(x)

def _sigmoid(x):
    return jax.nn.sigmoid(x)

def _layernorm(x, axis=-1, eps=1e-05):
    m = jnp.mean(x, axis=axis, keepdims=True)
    v = jnp.var(x, axis=axis, keepdims=True)
    return (x - m) / jnp.sqrt(v + eps)

def _scatter_add(tgt, idx, src, axis=0):
    return tgt.at[idx].add(src)

def _segment_sum(src, seg, n):
    return jax.ops.segment_sum(src, seg, n)
kernel_name = 'mk_xattn_seq_d4_seqx_r4_632dee'

def setup_inputs(seed: int=0):
    np.random.seed(seed)
    _w = jnp.asarray

    def _rec_inputs():
        import jax
        import jax.numpy as jnp
        _rk = jax.random.key(seed)
        x = -0.0005146 + 1 * jax.random.normal(jax.random.fold_in(_rk, 1), (16, 128, 512), jnp.float32)
        _lenS = 128 - jax.random.randint(jax.random.fold_in(_rk, 7), (16,), 0, max(1, 128 // 4) + 1, jnp.int32)
        _lenS2 = 128 - jax.random.randint(jax.random.fold_in(_rk, 8), (16,), 0, max(1, 128 // 4) + 1, jnp.int32)
        _ctx_2048P = jax.random.normal(jax.random.fold_in(_rk, 11), (16, 16, 512), jnp.float32)
        _ctx_2048c = jax.random.dirichlet(jax.random.fold_in(_rk, 511), 0.3 * jnp.ones((16,), jnp.float32), (16, 128))
        _ctx_2048t = jnp.einsum('bsk,bkd->bsd', _ctx_2048c, _ctx_2048P)
        _ctx_2048t = _ctx_2048t * jax.lax.rsqrt(jnp.mean(jnp.square(_ctx_2048t)) + 1e-12) * 0.953939
        ctx_2048 = -0.000392918 + 0.999932 * (_ctx_2048t + 0.3 * jax.random.normal(jax.random.fold_in(_rk, 611), (16, 128, 512), jnp.float32))
        _validS = jnp.arange(128)[None, :] < _lenS[:, None]
        _validS2 = jnp.arange(128)[None, :] < _lenS2[:, None]
        _causal = jnp.tril(jnp.ones((128, 128), dtype=bool))
        mask_BxS2_ik0 = jnp.where(jnp.broadcast_to(_validS2[:, :], (16, 128)), 0, 1).astype(jnp.int32)
        mask_Bx1xSxS2_ff0 = jnp.where(jnp.ones((16, 1, 128, 128), dtype=bool), 0.0, -1000000000.0).astype(jnp.float32)
        mask_BxS2_bf1 = jnp.ones((16, 128), dtype=bool)
        return (x, ctx_2048, mask_BxS2_ik0, mask_Bx1xSxS2_ff0, mask_BxS2_bf1)
    x, ctx_2048, mask_BxS2_ik0, mask_Bx1xSxS2_ff0, mask_BxS2_bf1 = _rec_inputs()

    def _L0_xattn_setup():
        import jax, jax.numpy as jnp
        import numpy as np
        B, P, K, H, NH = (4, 512, 64, 512, 16)
        DH = H // NH
        EPS = 1e-06

        def rmsnorm(x, w):
            var = jnp.mean(jnp.square(x), axis=-1, keepdims=True)
            return x * jax.lax.rsqrt(var + EPS) * w
        key = jax.random.key(seed)
        ks = jax.random.split(key, 12)
        s = 0.02
        return {'x': jax.random.normal(ks[0], (B, P, H), jnp.float32), 'latents': jax.random.normal(ks[1], (B, K, H), jnp.float32), 'attention_mask': jax.random.randint(ks[2], (B, P), 0, 2, jnp.int32), 'q_w': s * jax.random.normal(ks[3], (H, H), jnp.float32), 'q_b': jnp.zeros((H,), jnp.float32), 'kv_w': s * jax.random.normal(ks[4], (H, 2 * H), jnp.float32), 'kv_b': jnp.zeros((2 * H,), jnp.float32), 'out_w': s * jax.random.normal(ks[5], (H, H), jnp.float32), 'out_b': jnp.zeros((H,), jnp.float32), 'postnorm_w': jnp.ones((H,), jnp.float32), 'mlp_w1': s * jax.random.normal(ks[6], (H, 4 * H), jnp.float32), 'mlp_b1': jnp.zeros((4 * H,), jnp.float32), 'mlp_w2': s * jax.random.normal(ks[7], (4 * H, H), jnp.float32), 'mlp_b2': jnp.zeros((H,), jnp.float32)}
    _L0_xattn_all = _L0_xattn_setup()
    _L0_xattn_in = {k: v for k, v in _L0_xattn_all.items() if k in ('q_w', 'q_b', 'kv_w', 'kv_b', 'out_w', 'out_b', 'postnorm_w', 'mlp_w1', 'mlp_b1', 'mlp_w2', 'mlp_b2')}
    del _L0_xattn_all

    def _L1_xattn_setup():
        import jax, jax.numpy as jnp
        import numpy as np
        H = 512
        NH = 32
        KVH = 8
        HD = H // NH
        GROUPS = NH // KVH
        EPS = 1e-06
        B, L, S = (4, 256, 256)

        def _gqa_forward(hidden_state, encoder_hidden_state, encoder_attention_mask, Wq, bq, Wk, bk, Wv, bv, Wo, bo, gamma, beta):
            b, l, _ = hidden_state.shape
            s = encoder_hidden_state.shape[1]
            q = hidden_state @ Wq + bq
            k = encoder_hidden_state @ Wk + bk
            v = encoder_hidden_state @ Wv + bv
            q = q.reshape(b, l, KVH, GROUPS, HD).transpose(0, 2, 3, 1, 4)
            k = k.reshape(b, s, KVH, HD).transpose(0, 2, 1, 3)
            v = v.reshape(b, s, KVH, HD).transpose(0, 2, 1, 3)
            scale = 1.0 / jnp.sqrt(jnp.asarray(HD, q.dtype))
            scores = jnp.einsum('bkgld,bksd->bkgls', q, k) * scale
            scores = scores + encoder_attention_mask[:, :, None, :, :]
            attn = jax.nn.softmax(scores, axis=-1)
            out = jnp.einsum('bkgls,bksd->bkgld', attn, v)
            out = out.transpose(0, 3, 1, 2, 4).reshape(b, l, H)
            out = out @ Wo + bo
            x = out + hidden_state
            mu = jnp.mean(x, axis=-1, keepdims=True)
            var = jnp.var(x, axis=-1, keepdims=True)
            return (x - mu) * jax.lax.rsqrt(var + EPS) * gamma + beta
        key = jax.random.key(seed)
        ks = jax.random.split(key, 12)
        sd = 0.02
        return {'hidden_state': jax.random.normal(ks[0], (B, L, H), jnp.float32), 'encoder_hidden_state': jax.random.normal(ks[1], (B, S, H), jnp.float32), 'encoder_attention_mask': jnp.zeros((B, 1, L, S), jnp.float32), 'Wq': jax.random.normal(ks[2], (H, H), jnp.float32) * sd, 'bq': jnp.zeros((H,), jnp.float32), 'Wk': jax.random.normal(ks[3], (H, KVH * HD), jnp.float32) * sd, 'bk': jnp.zeros((KVH * HD,), jnp.float32), 'Wv': jax.random.normal(ks[4], (H, KVH * HD), jnp.float32) * sd, 'bv': jnp.zeros((KVH * HD,), jnp.float32), 'Wo': jax.random.normal(ks[5], (H, H), jnp.float32) * sd, 'bo': jnp.zeros((H,), jnp.float32), 'gamma': jnp.ones((H,), jnp.float32), 'beta': jnp.zeros((H,), jnp.float32)}
    _L1_xattn_all = _L1_xattn_setup()
    _L1_xattn_in = {k: v for k, v in _L1_xattn_all.items() if k in ('Wq', 'bq', 'Wk', 'bk', 'Wv', 'bv', 'Wo', 'bo', 'gamma', 'beta')}
    del _L1_xattn_all

    def _L2_xattn_setup():
        import jax, jax.numpy as jnp
        import numpy as np
        D = 512
        H = 16
        HD = D // H
        INNER = 4 * D
        EPS = 1e-05

        def layer_norm(x, w, b):
            mu = jnp.mean(x, axis=-1, keepdims=True)
            var = jnp.mean(jnp.square(x - mu), axis=-1, keepdims=True)
            return (x - mu) * jax.lax.rsqrt(var + EPS) * w + b
        key = jax.random.key(seed)
        ks = jax.random.split(key, 12)
        B, LQ, LK = (4, 256, 512)
        std = 0.02
        inp = {'hidden_states': jax.random.normal(ks[0], (B, LQ, D), jnp.float32), 'encoder_hidden_states': jax.random.normal(ks[1], (B, LK, D), jnp.float32), 'encoder_attention_mask': jnp.ones((B, LK), dtype=bool), 'ln1_w': jnp.ones((D,), jnp.float32), 'ln1_b': jnp.zeros((D,), jnp.float32), 'q_w': jax.random.normal(ks[2], (D, D), jnp.float32) * std, 'q_b': jnp.zeros((D,), jnp.float32), 'k_w': jax.random.normal(ks[3], (D, D), jnp.float32) * std, 'k_b': jnp.zeros((D,), jnp.float32), 'v_w': jax.random.normal(ks[4], (D, D), jnp.float32) * std, 'v_b': jnp.zeros((D,), jnp.float32), 'cproj_w': jax.random.normal(ks[5], (D, D), jnp.float32) * std, 'cproj_b': jnp.zeros((D,), jnp.float32), 'ln2_w': jnp.ones((D,), jnp.float32), 'ln2_b': jnp.zeros((D,), jnp.float32), 'fc_w': jax.random.normal(ks[6], (D, INNER), jnp.float32) * std, 'fc_b': jnp.zeros((INNER,), jnp.float32), 'proj_w': jax.random.normal(ks[7], (INNER, D), jnp.float32) * std, 'proj_b': jnp.zeros((D,), jnp.float32)}
        return inp
    _L2_xattn_all = _L2_xattn_setup()
    _L2_xattn_in = {k: v for k, v in _L2_xattn_all.items() if k in ('ln1_w', 'ln1_b', 'q_w', 'q_b', 'k_w', 'k_b', 'v_w', 'v_b', 'cproj_w', 'cproj_b', 'ln2_w', 'ln2_b', 'fc_w', 'fc_b', 'proj_w', 'proj_b')}
    del _L2_xattn_all

    def _L3_xattn_setup():
        import jax, jax.numpy as jnp
        import numpy as np
        B, P, K, H, NH = (4, 512, 64, 512, 16)
        DH = H // NH
        EPS = 1e-06

        def rmsnorm(x, w):
            var = jnp.mean(jnp.square(x), axis=-1, keepdims=True)
            return x * jax.lax.rsqrt(var + EPS) * w
        key = jax.random.key(seed)
        ks = jax.random.split(key, 12)
        s = 0.02
        return {'x': jax.random.normal(ks[0], (B, P, H), jnp.float32), 'latents': jax.random.normal(ks[1], (B, K, H), jnp.float32), 'attention_mask': jax.random.randint(ks[2], (B, P), 0, 2, jnp.int32), 'q_w': s * jax.random.normal(ks[3], (H, H), jnp.float32), 'q_b': jnp.zeros((H,), jnp.float32), 'kv_w': s * jax.random.normal(ks[4], (H, 2 * H), jnp.float32), 'kv_b': jnp.zeros((2 * H,), jnp.float32), 'out_w': s * jax.random.normal(ks[5], (H, H), jnp.float32), 'out_b': jnp.zeros((H,), jnp.float32), 'postnorm_w': jnp.ones((H,), jnp.float32), 'mlp_w1': s * jax.random.normal(ks[6], (H, 4 * H), jnp.float32), 'mlp_b1': jnp.zeros((4 * H,), jnp.float32), 'mlp_w2': s * jax.random.normal(ks[7], (4 * H, H), jnp.float32), 'mlp_b2': jnp.zeros((H,), jnp.float32)}
    _L3_xattn_all = _L3_xattn_setup()
    _L3_xattn_in = {k: v for k, v in _L3_xattn_all.items() if k in ('q_w', 'q_b', 'kv_w', 'kv_b', 'out_w', 'out_b', 'postnorm_w', 'mlp_w1', 'mlp_b1', 'mlp_w2', 'mlp_b2')}
    del _L3_xattn_all
    return {'x': x, 'ctx_2048': ctx_2048, 'mask_BxS2_ik0': mask_BxS2_ik0, 'mask_Bx1xSxS2_ff0': mask_Bx1xSxS2_ff0, 'mask_BxS2_bf1': mask_BxS2_bf1, 'L0_xattn_q_w': _L0_xattn_in['q_w'], 'L0_xattn_q_b': _L0_xattn_in['q_b'], 'L0_xattn_kv_w': _L0_xattn_in['kv_w'], 'L0_xattn_kv_b': _L0_xattn_in['kv_b'], 'L0_xattn_out_w': _L0_xattn_in['out_w'], 'L0_xattn_out_b': _L0_xattn_in['out_b'], 'L0_xattn_postnorm_w': _L0_xattn_in['postnorm_w'], 'L0_xattn_mlp_w1': _L0_xattn_in['mlp_w1'], 'L0_xattn_mlp_b1': _L0_xattn_in['mlp_b1'], 'L0_xattn_mlp_w2': _L0_xattn_in['mlp_w2'], 'L0_xattn_mlp_b2': _L0_xattn_in['mlp_b2'], 'L1_xattn_Wq': _L1_xattn_in['Wq'], 'L1_xattn_bq': _L1_xattn_in['bq'], 'L1_xattn_Wk': _L1_xattn_in['Wk'], 'L1_xattn_bk': _L1_xattn_in['bk'], 'L1_xattn_Wv': _L1_xattn_in['Wv'], 'L1_xattn_bv': _L1_xattn_in['bv'], 'L1_xattn_Wo': _L1_xattn_in['Wo'], 'L1_xattn_bo': _L1_xattn_in['bo'], 'L1_xattn_gamma': _L1_xattn_in['gamma'], 'L1_xattn_beta': _L1_xattn_in['beta'], 'L2_xattn_ln1_w': _L2_xattn_in['ln1_w'], 'L2_xattn_ln1_b': _L2_xattn_in['ln1_b'], 'L2_xattn_q_w': _L2_xattn_in['q_w'], 'L2_xattn_q_b': _L2_xattn_in['q_b'], 'L2_xattn_k_w': _L2_xattn_in['k_w'], 'L2_xattn_k_b': _L2_xattn_in['k_b'], 'L2_xattn_v_w': _L2_xattn_in['v_w'], 'L2_xattn_v_b': _L2_xattn_in['v_b'], 'L2_xattn_cproj_w': _L2_xattn_in['cproj_w'], 'L2_xattn_cproj_b': _L2_xattn_in['cproj_b'], 'L2_xattn_ln2_w': _L2_xattn_in['ln2_w'], 'L2_xattn_ln2_b': _L2_xattn_in['ln2_b'], 'L2_xattn_fc_w': _L2_xattn_in['fc_w'], 'L2_xattn_fc_b': _L2_xattn_in['fc_b'], 'L2_xattn_proj_w': _L2_xattn_in['proj_w'], 'L2_xattn_proj_b': _L2_xattn_in['proj_b'], 'L3_xattn_q_w': _L3_xattn_in['q_w'], 'L3_xattn_q_b': _L3_xattn_in['q_b'], 'L3_xattn_kv_w': _L3_xattn_in['kv_w'], 'L3_xattn_kv_b': _L3_xattn_in['kv_b'], 'L3_xattn_out_w': _L3_xattn_in['out_w'], 'L3_xattn_out_b': _L3_xattn_in['out_b'], 'L3_xattn_postnorm_w': _L3_xattn_in['postnorm_w'], 'L3_xattn_mlp_w1': _L3_xattn_in['mlp_w1'], 'L3_xattn_mlp_b1': _L3_xattn_in['mlp_b1'], 'L3_xattn_mlp_w2': _L3_xattn_in['mlp_w2'], 'L3_xattn_mlp_b2': _L3_xattn_in['mlp_b2']}

def reference(x, ctx_2048, mask_BxS2_ik0, mask_Bx1xSxS2_ff0, mask_BxS2_bf1, L0_xattn_q_w, L0_xattn_q_b, L0_xattn_kv_w, L0_xattn_kv_b, L0_xattn_out_w, L0_xattn_out_b, L0_xattn_postnorm_w, L0_xattn_mlp_w1, L0_xattn_mlp_b1, L0_xattn_mlp_w2, L0_xattn_mlp_b2, L1_xattn_Wq, L1_xattn_bq, L1_xattn_Wk, L1_xattn_bk, L1_xattn_Wv, L1_xattn_bv, L1_xattn_Wo, L1_xattn_bo, L1_xattn_gamma, L1_xattn_beta, L2_xattn_ln1_w, L2_xattn_ln1_b, L2_xattn_q_w, L2_xattn_q_b, L2_xattn_k_w, L2_xattn_k_b, L2_xattn_v_w, L2_xattn_v_b, L2_xattn_cproj_w, L2_xattn_cproj_b, L2_xattn_ln2_w, L2_xattn_ln2_b, L2_xattn_fc_w, L2_xattn_fc_b, L2_xattn_proj_w, L2_xattn_proj_b, L3_xattn_q_w, L3_xattn_q_b, L3_xattn_kv_w, L3_xattn_kv_b, L3_xattn_out_w, L3_xattn_out_b, L3_xattn_postnorm_w, L3_xattn_mlp_w1, L3_xattn_mlp_b1, L3_xattn_mlp_w2, L3_xattn_mlp_b2):
    import jax
    import jax.numpy as jnp

    def _L0_xattn_ref(x, latents, attention_mask, q_w, q_b, kv_w, kv_b, out_w, out_b, postnorm_w, mlp_w1, mlp_b1, mlp_w2, mlp_b2):
        import jax, jax.numpy as jnp
        import numpy as np
        B, P, K, H, NH = (4, 512, 64, 512, 16)
        DH = H // NH
        EPS = 1e-06

        def rmsnorm(x, w):
            var = jnp.mean(jnp.square(x), axis=-1, keepdims=True)
            return x * jax.lax.rsqrt(var + EPS) * w
        b, p, _ = x.shape
        k_len = latents.shape[1]
        residual = latents
        h = jnp.concatenate([x, latents], axis=1)
        q = (latents @ q_w + q_b).reshape(b, k_len, NH, DH)
        kv = (h @ kv_w + kv_b).reshape(b, p + k_len, NH, DH, 2)
        kmat, v = (kv[..., 0], kv[..., 1])
        attn = jnp.einsum('bkhd,bnhd->bhkn', q, kmat) / DH
        full_mask = jnp.concatenate([attention_mask.astype(bool), jnp.ones((b, k_len), bool)], axis=-1)
        attn = jnp.where(full_mask[:, None, None, :], attn, -jnp.inf)
        attn = jax.nn.softmax(attn.astype(jnp.float32), axis=-1).astype(q.dtype)
        attn_out = jnp.einsum('bhkn,bnhd->bkhd', attn, v).reshape(b, k_len, H)
        attn_out = attn_out @ out_w + out_b + residual
        out = rmsnorm(attn_out, postnorm_w)
        out = jax.nn.gelu(out @ mlp_w1 + mlp_b1) @ mlp_w2 + mlp_b2
        return out + residual

    def _L1_xattn_ref(hidden_state, encoder_hidden_state, encoder_attention_mask, Wq, bq, Wk, bk, Wv, bv, Wo, bo, gamma, beta):
        import jax, jax.numpy as jnp
        import numpy as np
        H = 512
        NH = 32
        KVH = 8
        HD = H // NH
        GROUPS = NH // KVH
        EPS = 1e-06
        B, L, S = (4, 256, 256)

        def _gqa_forward(hidden_state, encoder_hidden_state, encoder_attention_mask, Wq, bq, Wk, bk, Wv, bv, Wo, bo, gamma, beta):
            b, l, _ = hidden_state.shape
            s = encoder_hidden_state.shape[1]
            q = hidden_state @ Wq + bq
            k = encoder_hidden_state @ Wk + bk
            v = encoder_hidden_state @ Wv + bv
            q = q.reshape(b, l, KVH, GROUPS, HD).transpose(0, 2, 3, 1, 4)
            k = k.reshape(b, s, KVH, HD).transpose(0, 2, 1, 3)
            v = v.reshape(b, s, KVH, HD).transpose(0, 2, 1, 3)
            scale = 1.0 / jnp.sqrt(jnp.asarray(HD, q.dtype))
            scores = jnp.einsum('bkgld,bksd->bkgls', q, k) * scale
            scores = scores + encoder_attention_mask[:, :, None, :, :]
            attn = jax.nn.softmax(scores, axis=-1)
            out = jnp.einsum('bkgls,bksd->bkgld', attn, v)
            out = out.transpose(0, 3, 1, 2, 4).reshape(b, l, H)
            out = out @ Wo + bo
            x = out + hidden_state
            mu = jnp.mean(x, axis=-1, keepdims=True)
            var = jnp.var(x, axis=-1, keepdims=True)
            return (x - mu) * jax.lax.rsqrt(var + EPS) * gamma + beta
        return _gqa_forward(hidden_state, encoder_hidden_state, encoder_attention_mask, Wq, bq, Wk, bk, Wv, bv, Wo, bo, gamma, beta)

    def _L2_xattn_ref(hidden_states, encoder_hidden_states, encoder_attention_mask, ln1_w, ln1_b, q_w, q_b, k_w, k_b, v_w, v_b, cproj_w, cproj_b, ln2_w, ln2_b, fc_w, fc_b, proj_w, proj_b):
        import jax, jax.numpy as jnp
        import numpy as np
        D = 512
        H = 16
        HD = D // H
        INNER = 4 * D
        EPS = 1e-05

        def layer_norm(x, w, b):
            mu = jnp.mean(x, axis=-1, keepdims=True)
            var = jnp.mean(jnp.square(x - mu), axis=-1, keepdims=True)
            return (x - mu) * jax.lax.rsqrt(var + EPS) * w + b
        B, LQ, _ = hidden_states.shape
        LK = encoder_hidden_states.shape[1]
        residual = hidden_states
        x = layer_norm(hidden_states, ln1_w, ln1_b)
        q = (x @ q_w + q_b).reshape(B, LQ, H, HD).transpose(0, 2, 1, 3)
        k = (encoder_hidden_states @ k_w + k_b).reshape(B, LK, H, HD).transpose(0, 2, 1, 3)
        v = (encoder_hidden_states @ v_w + v_b).reshape(B, LK, H, HD).transpose(0, 2, 1, 3)
        scale = 1.0 / np.sqrt(HD).astype(np.float32)
        scores = jnp.einsum('bhqd,bhkd->bhqk', q, k) * scale
        mask = encoder_attention_mask[:, None, None, :]
        mask_value = jnp.finfo(scores.dtype).min
        scores = jnp.where(mask, scores, mask_value)
        attn = jax.nn.softmax(scores, axis=-1)
        out = jnp.einsum('bhqk,bhkd->bhqd', attn, v)
        out = out.transpose(0, 2, 1, 3).reshape(B, LQ, D)
        out = out @ cproj_w + cproj_b
        hidden = out + residual
        residual = hidden
        y = layer_norm(hidden, ln2_w, ln2_b)
        y = jax.nn.gelu(y @ fc_w + fc_b, approximate=True)
        y = y @ proj_w + proj_b
        return residual + y

    def _L3_xattn_ref(x, latents, attention_mask, q_w, q_b, kv_w, kv_b, out_w, out_b, postnorm_w, mlp_w1, mlp_b1, mlp_w2, mlp_b2):
        import jax, jax.numpy as jnp
        import numpy as np
        B, P, K, H, NH = (4, 512, 64, 512, 16)
        DH = H // NH
        EPS = 1e-06

        def rmsnorm(x, w):
            var = jnp.mean(jnp.square(x), axis=-1, keepdims=True)
            return x * jax.lax.rsqrt(var + EPS) * w
        b, p, _ = x.shape
        k_len = latents.shape[1]
        residual = latents
        h = jnp.concatenate([x, latents], axis=1)
        q = (latents @ q_w + q_b).reshape(b, k_len, NH, DH)
        kv = (h @ kv_w + kv_b).reshape(b, p + k_len, NH, DH, 2)
        kmat, v = (kv[..., 0], kv[..., 1])
        attn = jnp.einsum('bkhd,bnhd->bhkn', q, kmat) / DH
        full_mask = jnp.concatenate([attention_mask.astype(bool), jnp.ones((b, k_len), bool)], axis=-1)
        attn = jnp.where(full_mask[:, None, None, :], attn, -jnp.inf)
        attn = jax.nn.softmax(attn.astype(jnp.float32), axis=-1).astype(q.dtype)
        attn_out = jnp.einsum('bhkn,bnhd->bkhd', attn, v).reshape(b, k_len, H)
        attn_out = attn_out @ out_w + out_b + residual
        out = rmsnorm(attn_out, postnorm_w)
        out = jax.nn.gelu(out @ mlp_w1 + mlp_b1) @ mlp_w2 + mlp_b2
        return out + residual
    x = _L0_xattn_ref(ctx_2048, x, mask_BxS2_ik0, L0_xattn_q_w, L0_xattn_q_b, L0_xattn_kv_w, L0_xattn_kv_b, L0_xattn_out_w, L0_xattn_out_b, L0_xattn_postnorm_w, L0_xattn_mlp_w1, L0_xattn_mlp_b1, L0_xattn_mlp_w2, L0_xattn_mlp_b2)
    x = _L1_xattn_ref(x, ctx_2048, mask_Bx1xSxS2_ff0, L1_xattn_Wq, L1_xattn_bq, L1_xattn_Wk, L1_xattn_bk, L1_xattn_Wv, L1_xattn_bv, L1_xattn_Wo, L1_xattn_bo, L1_xattn_gamma, L1_xattn_beta)
    x = _L2_xattn_ref(x, ctx_2048, mask_BxS2_bf1, L2_xattn_ln1_w, L2_xattn_ln1_b, L2_xattn_q_w, L2_xattn_q_b, L2_xattn_k_w, L2_xattn_k_b, L2_xattn_v_w, L2_xattn_v_b, L2_xattn_cproj_w, L2_xattn_cproj_b, L2_xattn_ln2_w, L2_xattn_ln2_b, L2_xattn_fc_w, L2_xattn_fc_b, L2_xattn_proj_w, L2_xattn_proj_b)
    x = _L3_xattn_ref(ctx_2048, x, mask_BxS2_ik0, L3_xattn_q_w, L3_xattn_q_b, L3_xattn_kv_w, L3_xattn_kv_b, L3_xattn_out_w, L3_xattn_out_b, L3_xattn_postnorm_w, L3_xattn_mlp_w1, L3_xattn_mlp_b1, L3_xattn_mlp_w2, L3_xattn_mlp_b2)
    return x

_drawn_inputs = setup_inputs


def setup_inputs(seed=0):
    import zlib

    import numpy as np

    out = dict(_drawn_inputs(seed))
    spreads = {'L0_xattn_q_b': (0.0, 0.8),
     'L0_xattn_kv_b': (0.0, 0.8),
     'L0_xattn_out_b': (0.0, 1.157),
     'L0_xattn_postnorm_w': (1.0, 0.2),
     'L0_xattn_mlp_b1': (0.0, 0.1),
     'L0_xattn_mlp_b2': (0.0, 0.1),
     'L1_xattn_bq': (0.0, 0.8),
     'L1_xattn_bk': (0.0, 2.0),
     'L1_xattn_bv': (0.0, 0.1),
     'L1_xattn_bo': (0.0, 0.1),
     'L1_xattn_gamma': (1.0, 0.2),
     'L1_xattn_beta': (0.0, 0.1),
     'L2_xattn_ln1_w': (1.0, 0.6),
     'L2_xattn_ln1_b': (0.0, 0.8),
     'L2_xattn_q_b': (0.0, 0.8),
     'L2_xattn_k_b': (0.0, 2.0),
     'L2_xattn_v_b': (0.0, 0.1),
     'L2_xattn_cproj_b': (0.0, 0.1),
     'L2_xattn_ln2_w': (1.0, 0.2),
     'L2_xattn_ln2_b': (0.0, 0.375),
     'L2_xattn_fc_b': (0.0, 0.1),
     'L2_xattn_proj_b': (0.0, 0.1),
     'L3_xattn_q_b': (0.0, 2.0),
     'L3_xattn_kv_b': (0.0, 0.8),
     'L3_xattn_out_b': (0.0, 0.453),
     'L3_xattn_postnorm_w': (1.0, 0.2),
     'L3_xattn_mlp_b1': (0.0, 0.1),
     'L3_xattn_mlp_b2': (0.0, 0.1)}
    factors = {'L0_xattn_q_w': 8.0,
     'L0_xattn_kv_w': 8.0,
     'L0_xattn_out_w': 5.366,
     'L1_xattn_Wq': 8.0,
     'L1_xattn_Wk': 7.847,
     'L2_xattn_q_w': 7.807,
     'L2_xattn_k_w': 7.6,
     'L3_xattn_q_w': 8.0,
     'L3_xattn_kv_w': 5.075,
     'L3_xattn_out_w': 3.973}
    for name, (base, spread) in spreads.items():
        noise = np.random.default_rng([zlib.crc32(name.encode()), seed]).standard_normal(out[name].shape)
        drawn = base * np.exp(spread * noise) if base else spread * noise
        out[name] = jnp.asarray(drawn.astype(out[name].dtype))
    for name, factor in factors.items():
        out[name] = (out[name] * factor).astype(out[name].dtype)
    return out
```

```python
from contextlib import ExitStack

import numpy as np

import concourse.bass as bass
from concourse import mybir

ALU = mybir.AluOpType
ACT = mybir.ActivationFunctionType
AX = mybir.AxisListType
F32 = mybir.dt.float32
F32R = mybir.dt.float32r
BF16 = mybir.dt.bfloat16
I32 = mybir.dt.int32
U8 = mybir.dt.uint8

P = 128
B = 16
D = 512
FB = D // P
HID = 4 * D
NBLK = HID // P
ROWB = 4
GROUPS = B // ROWB
MASKED = -1e30

LATENT, GQA, CROSS = "latent", "gqa", "cross"


class Layer:

    def __init__(self, n, kind, weight_slot, mlp_slot, batches_before=0, groups_before=0, uses_before=0):
        self.n, self.kind = n, kind
        self.b0, self.g0, self.u0 = batches_before, groups_before, uses_before
        self.a0 = weight_slot
        self.m0 = mlp_slot
        self.mlp = kind != GQA
        self.rounds = 1 if kind == CROSS else 2
        self.width = 128 if kind == CROSS else 256
        self.segs = 2 if kind == LATENT else 4
        self.seg = D // self.segs
        self.scale = {LATENT: 1.0 / 32, GQA: 0.25, CROSS: float(np.float32(1.0) / np.sqrt(32).astype(np.float32))}[kind]
        self.eps = 1e-5 if kind == CROSS else 1e-6
        self.n_v = 2 if kind == LATENT else 1
        self.n_k = 1 if kind == GQA else 2
        self.k_cols = 256 if kind == LATENT else 128
        self.rings = {}
        n_use = self.u0
        for b in range(-2, B + 1):
            for name in self.slot_uses(b):
                self.rings[name, b] = n_use
                n_use += 1
        self.n_uses = n_use
        self.per_slot = self.rings["T0_0", 3] - self.rings["T0_0", 2]
        assert 2 * self.per_slot % 4 == 0
        for (name, b), at in self.rings.items():
            if 2 <= b and b + 2 <= B - 3:
                assert self.rings[name, b + 2] == at + 2 * self.per_slot

    def slot_uses(self, b):
        now, nxt, prev, far = 0 <= b < B, 0 <= b + 1 < B, 0 <= b - 1 < B, 0 <= b + 2 < B
        uses = []
        if nxt:
            uses += [f"K{i}" for i in range(self.n_k)]
        if prev:
            uses.append("out")
        if now and self.rounds == 2:
            uses += [f"T0_{r}" for r in range(4)] + ["O0"]
        if nxt:
            uses += ["Q"] + [f"V{i}" for i in range(self.n_v)]
        if far:
            uses += ["Xx", "Xc"]
        if now:
            s = self.rounds - 1
            uses += [f"T{s}_{r}" for r in range(4)] + [f"O{s}"]
        return uses


class Slot:

    def __init__(self, y, v, ref, turn):
        self.v, self.c, self.ref, self.turn = v, v + y.b0, ref, turn
        self.now, self.nxt = 0 <= ref < B, 0 <= ref + 1 < B
        self.prev, self.far = 0 <= ref - 1 < B, 0 <= ref + 2 < B
        self.par, self.par_next = ref % 2, (ref + 1) % 2


def over_slots(eng, y, slot):
    for b in range(-2, 2):
        slot(Slot(y, b, b, 0))
    with eng.Fori(0, (B - 4) // 2) as i:
        slot(Slot(y, i * 2 + 2, 2, i))
        slot(Slot(y, i * 2 + 3, 3, i))
    for b in range(B - 2, B + 1):
        slot(Slot(y, b, b, 0))


def wait(eng, sem, value):
    if isinstance(value, int) and value <= 0:
        return
    eng.wait_ge(sem, value)


def build(nc, ins, out):
    first = Layer(0, LATENT, 0, 8)
    L = [first, Layer(1, GQA, 8, 0), Layer(2, CROSS, 0, 8, groups_before=GROUPS),
         Layer(3, LATENT, 8, 0, B, 2 * GROUPS, first.n_uses)]
    ctx = ExitStack()
    with ctx:
        def sb(name, shape, dt):
            return ctx.enter_context(nc.sbuf_tensor(name, shape, dt))

        def sem(name):
            return ctx.enter_context(nc.semaphore(name))

        W = sb("weights", [P, 16, 2048], F32R)
        RR = sb("split_operands", [P, 9216], F32R)
        FF = sb("plain_operands", [P, 9472], F32)
        raw = sb("raw_weights", [P, 2, D], F32)
        ident = sb("ident", [P, P], F32)
        cols = sb("bias_columns", [P, 4, 44], F32)
        neg_max = sb("neg_max", [P, 4, 4], F32)
        row_sum = sb("row_sum", [P, 4, 4], F32)
        inv_sum = sb("inv_sum", [P, 4, 4], F32)
        stats = sb("stats", [P, 6], F32)
        moments = sb("moments", [P, 2], F32)
        spread = sb("spread", [P, 1], F32)
        spread_eps = sb("spread_eps", [P, 1], F32)
        neg_mean = sb("neg_mean", [P, 1], F32)
        rstd = sb("rstd", [P, 1], F32)
        minus_half = sb("minus_half", [P, 1], F32)
        even = sb("even", [P, 1], F32)
        odd = sb("odd", [P, 1], F32)
        first_row = sb("first_row", [P, P], BF16)
        mask_i32 = sb("mask_i32", [1, P], I32)
        mask_u8 = sb("mask_u8", [1, P], U8)

        def view(t, at, *shape):
            n = int(np.prod(shape))
            v = t[:, at:at + n]
            names = "abcd"[:len(shape)]
            return v.rearrange(f"p ({' '.join(names)}) -> p {' '.join(names)}", **dict(zip(names[1:], shape[1:]))) if len(shape) > 1 else v

        XC = view(RR, 0, 2, FB, 256)
        KT = [view(RR, 2048 + 2048 * h, 2, 4, 256) for h in range(2)]
        QT = [view(RR, 6144 + 1024 * h, 2, 4, P) for h in range(2)]
        OT = view(RR, 8192, 2, 4, P)
        x_nat, c_nat = view(FF, 0, D), view(FF, 512, D)
        V = [view(FF, 1024 + 1024 * h, 2, D) for h in range(2)]
        PR = view(FF, 3072, 4, D)
        PT = view(FF, 5120, 4, D)
        hidden, unit = view(FF, 7168, D), view(FF, 7680, D)
        out_bias, tmp = view(FF, 8192, D), view(FF, 8704, D)
        gamma, beta = V[0][:, 1, :], V[1][:, 1, :]
        qk_mask = view(FF, 9216, 2, P)
        mask_row = FF[:, 9216:9472].bitcast(BF16).rearrange("p (h n) -> p h n", h=2)
        UT = view(RR, 0, 2, FB, D)
        G = view(RR, 4096, 4, 2, D)
        u_nat, res = view(FF, 0, ROWB, D), view(FF, 2048, ROWB, D)
        gelu, affine = view(FF, 4096, 2, D), view(FF, 5120, 2, D)
        mlp_bias = view(FF, 6144, D)

        PS = ctx.enter_context(nc.psum_tensor("banks", [P, 8, D], F32))

        def rows(name):
            return nc.dram_tensor(name, [B, P, D], F32).ap()

        x_of = [ins["x"], rows("x1"), rows("x2"), rows("x3")]
        q_of = [x_of[0], x_of[1], rows("x2_unit"), x_of[3]]
        u_of = [rows("u0"), None, rows("u2"), rows("u3")]
        r_of = [x_of[0], None, rows("h2"), x_of[3]]
        y_of = [x_of[1], None, x_of[3], out]
        ctx_in = ins["ctx_2048"]

        def at_batch(t, v):
            return t[bass.ds(v, 1)].rearrange("a p n -> p (a n)")

        def at_group(t, v):
            return t.rearrange("(g r) p n -> g r p n", r=ROWB)[bass.ds(v, 1)].rearrange("a r p n -> p (a r) n")

        ident_zero, ident_done = sem("ident_zero"), sem("ident_done")
        consts, cols_loaded = sem("consts"), sem("cols_loaded")
        raw_loaded = [sem(f"raw_loaded{i}") for i in range(2)]
        passed = {e.engine: sem(f"passed_{n}") for n, e in (("pool", nc.gpsimd), ("dve", nc.vector), ("sp", nc.sync))}
        raw_scaled, tile_hi, tile_split = sem("raw_scaled"), sem("tile_hi"), sem("tile_split")

        class A:
            def __init__(self, l):
                s = lambda name: sem(f"a{l}_{name}")
                kind = L[l].kind
                self.x_loaded, self.c_loaded, self.res_loaded = s("x_loaded"), s("c_loaded"), s("res_loaded")
                self.mask_loaded, self.bias_loaded = s("mask_loaded"), s("bias_loaded")
                self.filled = s("filled")
                self.evacuated = [s(f"evacuated{k}") for k in range(4)]
                self.scored, self.maxed, self.exped = s("scored"), s("maxed"), s("exped")
                self.inverted, self.normed = s("inverted"), s("normed")
                self.x_hi, self.k_hi, self.q_hi, self.o_hi = s("x_hi"), s("k_hi"), s("q_hi"), s("o_hi")
                self.res_ready, self.moment_step, self.moments = s("res_ready"), s("moment_step"), s("moments")
                self.rstd_step, self.unit_ready, self.stored = s("rstd_step"), s("unit_ready"), s("stored")
                if kind != GQA:
                    self.mask_ready = s("mask_ready")
                self.zeroed = s("zeroed")
                if kind != LATENT:
                    self.stored2 = s("stored2")
                if kind == GQA:
                    self.mask_of = [s(f"mask_loaded_parity{h}") for h in range(2)]
                    self.summed, self.k_sum = s("mask_added"), s("k_sum")
                    self.scaled, self.norm_ready = s("scaled_by_gamma"), s("norm_ready")
                if kind == CROSS:
                    self.x_aff, self.x_aff_hi = s("x_affine"), s("x_affine_hi")

        class M:
            def __init__(self):
                s = lambda name: sem(f"m_{name}")
                self.u_loaded, self.res_loaded, self.bias_loaded = s("u_loaded"), s("res_loaded"), s("bias_loaded")
                self.turned, self.affined, self.ut_hi, self.ut_ready = s("turned"), s("affined"), s("ut_hi"), s("ut_ready")
                self.h_full, self.gelu_done, self.g_hi, self.g_ready = s("h_full"), s("gelu_done"), s("g_hi"), s("g_ready")
                self.y_step, self.res_ready, self.y_added = s("y_step"), s("res_ready"), s("y_added")
                self.stored = s("stored")

        As = [A(l) for l in range(3)]
        As.append(As[0])
        Ms = M()

        def hi_lo(slots, at, n):
            return W[:, slots, at:at + n]

        def attention_tiles(y):
            w = lambda i: W[:, y.a0 + i, :]
            tiles = []
            p = f"L{y.n}_xattn_"
            half = lambda f: slice(f * P, f * P + P)

            def plain(name, i_hi, i_lo, scale=None):
                for f in range(FB):
                    tiles.append((ins[p + name][half(f), :], lambda t: t,
                                  w(i_hi)[:, f * D:(f + 1) * D], w(i_lo)[:, f * D:(f + 1) * D], scale))

            plain({GQA: "Wq"}.get(y.kind, "q_w"), 0, 1, y.scale)
            if y.kind == LATENT:
                for f in range(FB):
                    for c in range(2):
                        at = f * D + c * 256
                        tiles.append((ins[p + "kv_w"][half(f), c * D:(c + 1) * D],
                                      lambda t: t.rearrange("p (n two) -> p two n", two=2),
                                      W[:, y.a0 + 2:y.a0 + 4, at:at + 256], W[:, y.a0 + 4:y.a0 + 6, at:at + 256], None))
            elif y.kind == CROSS:
                plain("k_w", 2, 4)
                plain("v_w", 3, 5)
            else:
                for f in range(FB):
                    rep = lambda s, f=f: w(s)[:, f * D:(f + 1) * D].rearrange("p (j r d) -> p j r d", r=4, d=16)
                    tiles.append((ins[p + "Wk"][half(f), :],
                                  lambda t: t[:, 0:P].rearrange("p (j d) -> p j d", d=16).unsqueeze(2).broadcast_to([P, 8, 4, 16]),
                                  rep(2), rep(4), None))
                for f in range(FB):
                    tiles.append((ins[p + "Wv"][half(f), :], lambda t: t[:, 0:P],
                                  w(3)[:, f * P:(f + 1) * P], w(5)[:, f * P:(f + 1) * P], None))
            plain({GQA: "Wo", CROSS: "cproj_w"}.get(y.kind, "out_w"), 6, 7)
            return tiles

        def mlp_tiles(y):
            p = f"L{y.n}_xattn_"
            w1, w2 = (ins[p + n] for n in (("fc_w", "proj_w") if y.kind == CROSS else ("mlp_w1", "mlp_w2")))
            tiles = []
            for j in range(NBLK):
                s = (y.m0 + j) % 16
                tiles.append((w1.rearrange("(f p) n -> p f n", p=P)[:, :, j * P:(j + 1) * P], lambda t: t,
                              W[:, s, 0:D], W[:, s, D:2 * D], None))
                tiles.append((w2[j * P:(j + 1) * P, :], lambda t: t, W[:, s, 2 * D:3 * D], W[:, s, 3 * D:4 * D], None))
            return tiles

        phases, first_tile, n_tiles, n_scaled = {}, {}, 0, 0
        for y in L:
            for key, tiles in [(("a", y.n), attention_tiles(y))] + ([(("m", y.n), mlp_tiles(y))] if y.mlp else []):
                phases[key], first_tile[key] = tiles, (n_tiles, n_scaled)
                n_tiles += len(tiles)
                n_scaled += sum(t[4] is not None for t in tiles)

        def load_tile(sp, key, i):
            n = first_tile[key][0] + i
            src = phases[key][i][0]
            wait(sp, tile_split, n - 1)
            dst = raw[:, n % 2, :]
            if len(src.shape) == 3:
                dst = dst.rearrange("p (f n) -> p f n", f=FB)
            else:
                dst = dst[:, 0:src.shape[1]]
            sp.dma_start(dst, src).then_inc(raw_loaded[n % 2], 16)

        def split_tile(pool, key, i):
            n = first_tile[key][0] + i
            src, pick, hi, lo, scale = phases[key][i]
            buf = raw[:, n % 2, :]
            pool.wait_ge(raw_loaded[n % 2], 16 * (n // 2 + 1))
            if scale is not None:
                m = first_tile[key][1] + sum(t[4] is not None for t in phases[key][:i]) + 1
                pool.tensor_scalar(buf, buf, scale, 1.0, ALU.mult, ALU.mult).then_inc(raw_scaled, 1)
                pool.wait_ge(raw_scaled, m)
            v = pick(buf)
            pool.tensor_copy(hi, v).then_inc(tile_hi, 1)
            pool.wait_ge(tile_hi, n + 1)
            pool.tensor_tensor(lo, v, hi.bitcast(F32), ALU.subtract).then_inc(tile_split, 1)

        def tiles_ready(pe, key, i):
            pe.wait_ge(tile_split, first_tile[key][0] + i + 1)

        def settled(eng):
            eng.sem_inc(passed[eng.engine], 1)

        def ring(y, sl, name, back=0):
            n0 = y.rings[name, sl.ref - back]
            step = 2 * y.per_slot
            return n0 % 4, sl.turn * (step // 4) + n0 // 4 + 1, sl.turn * step + n0 + 1

        def wait_evacuated(eng, y, sl, name, back=0):
            k, count, _ = ring(y, sl, name, back)
            eng.wait_ge(As[y.n].evacuated[k], count)

        def wait_filled(eng, y, sl, name, back=0):
            eng.wait_ge(As[y.n].filled, ring(y, sl, name, back)[2])

        def bank(y, sl, name):
            return PS[:, 4 + ring(y, sl, name)[0], :]

        def step_of(y, sl, s, r):
            return sl.c * (4 * y.rounds) + (4 * s + r + 1)

        Y_STEPS = NBLK - 1 + ROWB

        def sp_attention(sp, y):
            a, p = As[y.n], f"L{y.n}_xattn_"
            if y.n:
                wait_phase_before(sp, y)
            bias = {GQA: "bo", CROSS: "cproj_b"}.get(y.kind, "out_b")
            wide = lambda name: ins[p + name].rearrange("(a n) -> a n", a=1).broadcast_to([P, D])
            sp.dma_start(out_bias, wide(bias)).then_inc(a.bias_loaded, 16)
            if y.kind == GQA:
                sp.dma_start(gamma, wide("gamma")).then_inc(a.bias_loaded, 16)
                sp.dma_start(beta, wide("beta")).then_inc(a.bias_loaded, 16)

            def slot(sl):
                if sl.far:
                    if sl.ref > -2:
                        wait_filled(sp, y, sl, "Xc", 1)
                    sp.dma_start(x_nat, at_batch(q_of[y.n], sl.v + 2)).then_inc(a.x_loaded, 16)
                    sp.dma_start(c_nat, at_batch(ctx_in, sl.v + 2)).then_inc(a.c_loaded, 16)
                if sl.nxt:
                    if y.kind == GQA:
                        wait(sp, a.summed, sl.c * 8)
                        sp.dma_start(qk_mask[:, sl.par_next, :],
                                     ins["mask_Bx1xSxS2_ff0"].rearrange("b o q k -> b (o q) k")[bass.ds(sl.v + 1, 1)]
                                     .rearrange("a p n -> p (a n)")).then_inc(a.mask_of[sl.par_next], 16)
                    else:
                        wait(sp, a.mask_ready, sl.c + 1)
                        settled(sp)
                        src, dst = ((ins["mask_BxS2_bf1"], mask_u8) if y.kind == CROSS else (ins["mask_BxS2_ik0"], mask_i32))
                        sp.dma_start(dst[0:1, :], src[bass.ds(sl.v + 1, 1), :]).then_inc(a.mask_loaded, 16)
                if sl.prev:
                    if y.kind == GQA:
                        sp.wait_ge(a.norm_ready, sl.c)
                        sp.dma_start(at_batch(x_of[2], sl.v - 1), hidden).then_inc(a.stored2, 16)
                    sp.wait_ge(a.unit_ready, sl.c)
                    sp.dma_start(at_batch(q_of[2] if y.kind == GQA else u_of[y.n], sl.v - 1), unit).then_inc(a.stored, 16)
                    if y.kind == CROSS:
                        sp.dma_start(at_batch(r_of[2], sl.v - 1), hidden).then_inc(a.stored2, 16)
                if sl.now:
                    if y.kind != LATENT:
                        wait(sp, a.stored2, sl.c * 16)
                    sp.dma_start(hidden, at_batch(x_of[y.n], sl.v)).then_inc(a.res_loaded, 16)

            over_slots(sp, y, slot)
            sp.wait_ge(a.stored, 16 * (y.b0 + B))
            if y.kind != LATENT:
                sp.wait_ge(a.stored2, 16 * (y.b0 + B))

        def wait_phase_before(eng, y):
            if L[y.n - 1].mlp:
                eng.wait_ge(Ms.stored, 16 * (L[y.n - 1].g0 + GROUPS))
            else:
                eng.wait_ge(As[y.n - 1].stored, 16 * B)
                eng.wait_ge(As[y.n - 1].stored2, 16 * B)

        def sp_mlp(sp, y):
            m, p = Ms, f"L{y.n}_xattn_"
            sp.dma_start(mlp_bias, ins[p + ("proj_b" if y.kind == CROSS else "mlp_b2")]
                         .rearrange("(a n) -> a n", a=1).broadcast_to([P, D])).then_inc(m.bias_loaded, 16)

            def load_u(i, g):
                if not isinstance(g, int) or g:
                    sp.wait_ge(m.turned, g * FB)
                sp.dma_start(u_nat, at_group(u_of[y.n], i)).then_inc(m.u_loaded, 16)

            def load_res(i, g):
                if not isinstance(g, int) or g:
                    sp.wait_ge(m.stored, g * 16)
                sp.dma_start(res, at_group(r_of[y.n], i)).then_inc(m.res_loaded, 16)

            def store(i, g):
                sp.wait_ge(m.y_added, g * ROWB + ROWB)
                sp.dma_start(at_group(y_of[y.n], i), res).then_inc(m.stored, 16)

            def turn_over(i, g):
                load_u(i + 1, g + 1)
                store(i, g)
                load_res(i + 1, g + 1)

            load_u(0, y.g0)
            load_res(0, y.g0)
            for i in range(len(phases["m", y.n])):
                load_tile(sp, ("m", y.n), i)
            turn_over(0, y.g0)
            with sp.Fori(1, GROUPS - 1) as i:
                turn_over(i, i + y.g0)
            if y.n < 3:
                for i in range(len(phases["a", y.n + 1])):
                    load_tile(sp, ("a", y.n + 1), i)
            store(GROUPS - 1, y.g0 + GROUPS - 1)
            if y.n == 3:
                sp.wait_ge(m.stored, 16 * (y.g0 + GROUPS))

        def pool_attention(pool, y):
            a = As[y.n]
            if y.kind == GQA:
                wait_phase_before(pool, y)
                pool.memset(V[0][:, 0, :], 0.0).then_inc(a.zeroed, 1)
                pool.memset(V[1][:, 0, :], 0.0).then_inc(a.zeroed, 1)

            def softmax_norm(sl, s):
                for r in range(4):
                    pool.wait_ge(a.inverted, step_of(y, sl, s, r))
                    settled(pool)
                    for g in range(y.segs):
                        part = PR[:, r, g * y.seg:(g + 1) * y.seg]
                        ins_ = pool.tensor_scalar(part, part, inv_sum[:, r, g:g + 1], 1.0, ALU.mult, ALU.mult)
                    ins_.then_inc(a.normed, 1)

            def slot(sl):
                if sl.prev:
                    pool.wait_ge(a.res_loaded, sl.c * 16)
                    if sl.ref == 1:
                        pool.wait_ge(a.bias_loaded, 48 if y.kind == GQA else 32 if y.b0 else 16)
                    pool.tensor_tensor(hidden, hidden, out_bias, ALU.add).then_inc(a.res_ready, 1)
                if sl.now:
                    softmax_norm(sl, 0)
                if sl.prev:
                    n_steps = 5 if y.kind == GQA else 2
                    base = (sl.c - 1) * n_steps

                    def root(n, k):
                        pool.wait_ge(a.moments, n)
                        settled(pool)
                        eps = y.eps if k == 0 else L[2].eps
                        pool.tensor_scalar(spread_eps[:], spread[:], eps, 1.0, ALU.add, ALU.mult).then_inc(a.rstd_step, 1)
                        pool.wait_ge(a.rstd_step, base + (1 if k == 0 else 4))
                        pool.tensor_tensor(rstd[:], spread_eps[:], minus_half[:], ALU.pow).then_inc(a.rstd_step, 1)
                        pool.wait_ge(a.rstd_step, base + (2 if k == 0 else 5))
                        settled(pool)

                    if y.kind == GQA:
                        root(sl.c * 2 - 1, 0)
                        wait(pool, a.stored, (sl.c - 1) * 16)
                        settled(pool)
                        pool.tensor_scalar(unit, hidden, neg_mean[:, 0:1], rstd[:, 0:1], ALU.add, ALU.mult).then_inc(a.rstd_step, 1)
                        pool.wait_ge(a.rstd_step, base + 3)
                        pool.tensor_tensor(unit, unit, gamma, ALU.mult).then_inc(a.scaled, 1)
                        pool.wait_ge(a.scaled, sl.c)
                        pool.tensor_tensor(hidden, unit, beta, ALU.add).then_inc(a.norm_ready, 1)
                        root(sl.c * 2, 1)
                        pool.tensor_scalar(unit, hidden, neg_mean[:, 0:1], rstd[:, 0:1], ALU.add, ALU.mult).then_inc(a.unit_ready, 1)
                    else:
                        root(sl.c, 0)
                        wait(pool, a.stored, (sl.c - 1) * 16)
                        settled(pool)
                        first, op = (neg_mean[:, 0:1], ALU.add) if y.kind == CROSS else (1.0, ALU.mult)
                        pool.tensor_scalar(unit, hidden, first, rstd[:, 0:1], op, ALU.mult).then_inc(a.unit_ready, 1)
                if sl.now and y.rounds == 2:
                    softmax_norm(sl, 1)

            over_slots(pool, y, slot)

        def pool_mlp(pool, y):
            m = Ms

            def add_bias(g):
                pool.wait_ge(m.res_loaded, g * 16 + 16)
                for r in range(ROWB):
                    last = pool.tensor_tensor(res[:, r, :], res[:, r, :], mlp_bias, ALU.add)
                last.then_inc(m.res_ready, 1)

            pool.wait_ge(m.bias_loaded, 16 * (y.g0 // GROUPS + 1))
            add_bias(y.g0)
            pool.wait_ge(As[y.n].filled, y.n_uses)
            for i in range(len(phases["m", y.n])):
                split_tile(pool, ("m", y.n), i)
            with pool.Fori(1, GROUPS) as i:
                add_bias(i + y.g0)
            if y.n < 3:
                pool.wait_ge(m.y_step, (y.g0 + GROUPS - 1) * Y_STEPS + 8)
                for i in range(len(phases["a", y.n + 1])):
                    split_tile(pool, ("a", y.n + 1), i)

        def act_attention(act, y):
            a = As[y.n]
            c = lambda i: cols[:, y.n, i:i + 1]
            act.wait_ge(consts, N_CONSTS)

            def exps(sl, s):
                for r in range(4):
                    act.wait_ge(a.maxed, step_of(y, sl, s, r))
                    if y.kind != GQA and (sl.ref > 0 or s > 0):
                        if s > 0:
                            wait_filled(act, y, sl, f"T{s - 1}_{r}")
                        else:
                            wait_filled(act, y, sl, f"T{y.rounds - 1}_{r}", 1)
                    for g in range(y.segs):
                        part = slice(g * y.seg, (g + 1) * y.seg)
                        src = PR[:, r, part] if y.kind == GQA else PS[:, r, part]
                        last = act.activation(PR[:, r, part], src, ACT.Exp, bias=neg_max[:, r, g:g + 1],
                                              accum_out=row_sum[:, r, g:g + 1])
                    last.then_inc(a.exped, 1)

            def turn(sl, s):
                for r in (0, 2):
                    name = f"T{s}_{r}"
                    wait_filled(act, y, sl, name)
                    act.activation(PT[:, r, :], bank(y, sl, name), ACT.Copy).then_inc(a.evacuated[ring(y, sl, name)[0]], 1)
                name = f"O{s}"
                wait_filled(act, y, sl, name)
                n = 4 // y.rounds
                for i in range(n):
                    blk = n * s + i
                    last = act.activation(OT[:, 0, blk, :], bank(y, sl, name)[:, i * P:(i + 1) * P], ACT.Identity,
                                          bias=c(8 + blk))
                last.then_inc(a.o_hi, 1)

            def keys(sl):
                if y.kind == GQA:
                    act.wait_ge(a.k_sum, sl.c + 2)
                    four = lambda t: t.rearrange("p (t n) -> p t n", t=4)
                    act.activation(KT[sl.par_next][:, 0, :, 0:P], four(tmp), ACT.Copy, scale=even[:, 0:1])
                    act.activation(KT[sl.par_next][:, 0, :, P:2 * P], four(tmp), ACT.Copy, scale=odd[:, 0:1]).then_inc(a.k_hi, 1)
                    return
                for i in range(2):
                    wait_filled(act, y, sl, f"K{i}")
                    for j in range(2):
                        n = y.k_cols
                        last = act.activation(KT[sl.par_next][:, 0, 2 * i + j, 0:n], bank(y, sl, f"K{i}")[:, j * n:(j + 1) * n],
                                              ACT.Identity, bias=c(4 + 2 * i + j))
                    last.then_inc(a.k_hi, 1)

            def slot(sl):
                if sl.now:
                    exps(sl, 0)
                if sl.nxt:
                    keys(sl)
                if sl.now and y.rounds == 2:
                    turn(sl, 0)
                    exps(sl, 1)
                if sl.nxt:
                    wait_filled(act, y, sl, "Q")
                    for j in range(4):
                        last = act.activation(QT[sl.par_next][:, 0, j, :], bank(y, sl, "Q")[:, j * P:(j + 1) * P],
                                              ACT.Identity, bias=c(j))
                    last.then_inc(a.q_hi, 1)
                    wait_filled(act, y, sl, "V0")
                    if y.kind == GQA:
                        if sl.ref == -1:
                            act.wait_ge(a.zeroed, 2)
                        heads = bank(y, sl, "V0")[:, 0:P].rearrange("p (j d) -> p j d", d=16)
                        pairs = V[sl.par_next][:, 0, :].rearrange("p (j a n) -> p j a n", a=2, n=32)
                        act.activation(pairs[:, :, 0, 0:16], heads, ACT.Copy)
                        last = act.activation(pairs[:, :, 1, 16:32], heads, ACT.Copy)
                    else:
                        last = act.activation(V[sl.par_next][:, 0, :], bank(y, sl, "V0"), ACT.Copy)
                    last.then_inc(a.evacuated[ring(y, sl, "V0")[0]], 1)
                if sl.far:
                    wait_filled(act, y, sl, "Xx")
                    if y.kind == CROSS:
                        for f in range(FB):
                            last = act.activation(tmp[:, f * P:(f + 1) * P], bank(y, sl, "Xx")[:, f * P:(f + 1) * P],
                                                  ACT.Identity, bias=c(24 + f), scale=c(20 + f))
                        last.then_inc(a.x_aff, 1)
                    else:
                        act.activation(XC[:, 0, :, P:2 * P], bank(y, sl, "Xx").rearrange("p (f n) -> p f n", f=FB),
                                       ACT.Copy).then_inc(a.x_hi, 1)
                    wait_filled(act, y, sl, "Xc")
                    act.activation(XC[:, 0, :, 0:P], bank(y, sl, "Xc").rearrange("p (f n) -> p f n", f=FB),
                                   ACT.Copy).then_inc(a.x_hi, 1)
                if sl.now:
                    turn(sl, y.rounds - 1)

            over_slots(act, y, slot)

        def act_mlp(act, y):
            m = Ms
            c = lambda i: cols[:, y.n, i:i + 1]

            def affines(g):
                for f in range(FB):
                    act.wait_ge(m.turned, g * FB + (f + 1))
                    wait(act, m.ut_ready, g * FB + (f - 1))
                    act.activation(affine[:, f % 2, :], PS[:, 6 + f % 2, :], ACT.Identity,
                                   bias=c(16 + f) if y.kind == CROSS else 0.0, scale=c(12 + f)).then_inc(m.affined, 1)

            def group(g, more):
                for j in range(NBLK):
                    act.wait_ge(m.h_full, g * NBLK + (j + 1))
                    wait(act, m.g_ready, g * NBLK + (j - 1))
                    act.activation(gelu[:, j % 2, :], PS[:, 4 + j % 2, :], ACT.Gelu_apprx_tanh,
                                   bias=c(28 + j)).then_inc(m.gelu_done, 1)
                if more:
                    affines(g + 1)

            affines(y.g0)
            group(y.g0, True)
            with act.Fori(1, GROUPS - 1) as i:
                group(i + y.g0, True)
            group(y.g0 + GROUPS - 1, False)

        def dve_attention(dve, y):
            a = As[y.n]
            c = lambda i: cols[:, y.n, i:i + 1]
            dve.wait_ge(consts, N_CONSTS)

            def scores(sl, s):
                for r in range(4):
                    dve.wait_ge(a.scored, step_of(y, sl, s, r))
                    src = PS[:, r, :]
                    if y.kind == GQA:
                        if s > 0:
                            wait_filled(dve, y, sl, f"T{s - 1}_{r}")
                        elif sl.ref > 0:
                            wait_filled(dve, y, sl, f"T{y.rounds - 1}_{r}", 1)
                        if s == 0 and r == 0:
                            dve.wait_ge(a.mask_of[sl.par], sl.turn * 16 + 16 * (sl.ref // 2 + 1))
                        dve.tensor_tensor(PR[:, r, :].rearrange("p (u n) -> p u n", u=4), src.rearrange("p (u n) -> p u n", u=4),
                                          qk_mask[:, sl.par, :].unsqueeze(1).broadcast_to([P, 4, P]), ALU.add).then_inc(a.summed, 1)
                        dve.wait_ge(a.summed, step_of(y, sl, s, r))
                        src = PR[:, r, :]
                    dve.tensor_reduce(neg_max[:, r, 0:y.segs], src.rearrange("p (g n) -> p g n", g=y.segs), AX.X, ALU.max,
                                      negate=True).then_inc(a.maxed, 1)
                for r in range(4):
                    dve.wait_ge(a.exped, step_of(y, sl, s, r))
                    dve.reciprocal(inv_sum[:, r, 0:y.segs], row_sum[:, r, 0:y.segs]).then_inc(a.inverted, 1)

            def turn(sl, s):
                for r in (1, 3):
                    name = f"T{s}_{r}"
                    wait_filled(dve, y, sl, name)
                    dve.tensor_copy(PT[:, r, :], bank(y, sl, name)).then_inc(a.evacuated[ring(y, sl, name)[0]], 1)
                name = f"O{s}"
                dve.wait_ge(a.o_hi, sl.c * y.rounds + (s + 1))
                n = 4 // y.rounds
                for i in range(n):
                    blk = n * s + i
                    last = dve.scalar_tensor_tensor(out=OT[:, 1, blk, :], in0=bank(y, sl, name)[:, i * P:(i + 1) * P], scalar=c(8 + blk),
                                                    in1=OT[:, 0, blk, :].bitcast(F32), op0=ALU.add, op1=ALU.subtract)
                last.then_inc(a.evacuated[ring(y, sl, name)[0]], 1)

            def keys(sl):
                if y.kind == GQA:
                    wait_filled(dve, y, sl, "K0")
                    four = lambda t: t.rearrange("p (t n) -> p t n", t=4)
                    dve.tensor_tensor(four(tmp), four(bank(y, sl, "K0")), cols[:, y.n, 4:8].unsqueeze(2).broadcast_to([P, 4, P]),
                                      ALU.add).then_inc(a.k_sum, 1)
                    dve.wait_ge(a.k_hi, sl.c + 2)
                    for i, keep in enumerate((even, odd)):
                        dst = KT[sl.par_next][:, :, :, i * P:(i + 1) * P]
                        last = dve.scalar_tensor_tensor(out=dst[:, 1], in0=four(tmp), scalar=keep[:, 0:1], in1=dst[:, 0].bitcast(F32),
                                                        op0=ALU.mult, op1=ALU.subtract)
                    last.then_inc(a.evacuated[ring(y, sl, "K0")[0]], 1)
                    return
                for i in range(2):
                    dve.wait_ge(a.k_hi, sl.c * 2 + (2 + i + 1))
                    for j in range(2):
                        n, t = y.k_cols, 2 * i + j
                        last = dve.scalar_tensor_tensor(out=KT[sl.par_next][:, 1, t, 0:n], in0=bank(y, sl, f"K{i}")[:, j * n:(j + 1) * n],
                                                        scalar=c(4 + t), in1=KT[sl.par_next][:, 0, t, 0:n].bitcast(F32),
                                                        op0=ALU.add, op1=ALU.subtract)
                    last.then_inc(a.evacuated[ring(y, sl, f"K{i}")[0]], 1)

            def moments_of(n, n_step):
                dve.bn_stats(stats[:, :], hidden).then_inc(a.moment_step, 1)
                dve.wait_ge(a.moment_step, n_step + 1)
                settled(dve)
                dve.bn_aggr(moments[:, :], stats[:, :]).then_inc(a.moment_step, 1)
                dve.wait_ge(a.moment_step, n_step + 2)
                if y.kind == LATENT:
                    dve.scalar_tensor_tensor(out=spread[:, :], in0=moments[:, 0:1], scalar=moments[:, 0:1], in1=moments[:, 1:2],
                                             op0=ALU.mult, op1=ALU.add).then_inc(a.moments, 1)
                else:
                    dve.tensor_scalar(neg_mean[:, :], moments[:, 0:1], -1.0, None, ALU.mult)
                    dve.tensor_copy(spread[:, :], moments[:, 1:2]).then_inc(a.moments, 1)

            def masks(sl):
                dve.wait_ge(a.mask_loaded, sl.c * 16 + 32)
                src = mask_u8 if y.kind == CROSS else mask_i32
                dve.tensor_scalar(mask_row[0:1, sl.par_next, 0:P], src[0:1, :], 0.0, MASKED, ALU.is_equal, ALU.mult).then_inc(a.mask_ready, 1)

            def slot(sl):
                if sl.nxt and y.kind != GQA and sl.ref == -1:
                    dve.wait_ge(a.x_loaded, 16 * (y.b0 + 1))
                    dve.memset(FF[:, 9216:9472], 0.0).then_inc(a.zeroed, 1)
                    dve.wait_ge(a.zeroed, 2 if y.b0 else 1)
                    masks(sl)
                if sl.now:
                    scores(sl, 0)
                if sl.nxt:
                    keys(sl)
                if sl.prev:
                    wait_filled(dve, y, sl, "out")
                    dve.wait_ge(a.res_ready, sl.c)
                    k, count, _ = ring(y, sl, "out")
                    dve.tensor_tensor(hidden, bank(y, sl, "out"), hidden, ALU.add).then_inc(a.evacuated[k], 1)
                    dve.wait_ge(a.evacuated[k], count)
                    wait(dve, a.unit_ready, sl.c - 1)
                    moments_of(None, (sl.c - 1) * (4 if y.kind == GQA else 2))
                if sl.now and y.rounds == 2:
                    turn(sl, 0)
                    if sl.prev and y.kind == GQA:
                        dve.wait_ge(a.norm_ready, sl.c)
                        moments_of(None, (sl.c - 1) * 4 + 2)
                    scores(sl, 1)
                elif sl.prev and y.kind == GQA:
                    dve.wait_ge(a.norm_ready, sl.c)
                    moments_of(None, (sl.c - 1) * 4 + 2)
                if sl.nxt:
                    if y.kind != GQA and sl.ref >= 0:
                        masks(sl)
                    dve.wait_ge(a.q_hi, sl.c + 2)
                    for j in range(4):
                        last = dve.scalar_tensor_tensor(out=QT[sl.par_next][:, 1, j, :], in0=bank(y, sl, "Q")[:, j * P:(j + 1) * P],
                                                        scalar=c(j), in1=QT[sl.par_next][:, 0, j, :].bitcast(F32),
                                                        op0=ALU.add, op1=ALU.subtract)
                    last.then_inc(a.evacuated[ring(y, sl, "Q")[0]], 1)
                    if y.n_v == 2:
                        wait_filled(dve, y, sl, "V1")
                        dve.tensor_copy(V[sl.par_next][:, 1, :], bank(y, sl, "V1")).then_inc(a.evacuated[ring(y, sl, "V1")[0]], 1)
                if sl.far:
                    per_x = 1 if y.kind == CROSS else 2
                    if y.kind == CROSS:
                        dve.wait_ge(a.x_aff, sl.c + 3)
                        four = tmp.rearrange("p (f n) -> p f n", f=FB)
                        dve.tensor_copy(XC[:, 0, :, P:2 * P], four).then_inc(a.x_aff_hi, 1)
                        dve.wait_ge(a.x_aff_hi, sl.c + 3)
                        dve.tensor_tensor(XC[:, 1, :, P:2 * P], four, XC[:, 0, :, P:2 * P].bitcast(F32),
                                          ALU.subtract).then_inc(a.evacuated[ring(y, sl, "Xx")[0]], 1)
                    else:
                        dve.wait_ge(a.x_hi, sl.c * 2 + 5)
                        dve.tensor_tensor(XC[:, 1, :, P:2 * P], bank(y, sl, "Xx").rearrange("p (f n) -> p f n", f=FB),
                                          XC[:, 0, :, P:2 * P].bitcast(F32), ALU.subtract).then_inc(a.evacuated[ring(y, sl, "Xx")[0]], 1)
                    dve.wait_ge(a.x_hi, sl.c * per_x + (3 * per_x))
                    dve.tensor_tensor(XC[:, 1, :, 0:P], bank(y, sl, "Xc").rearrange("p (f n) -> p f n", f=FB),
                                      XC[:, 0, :, 0:P].bitcast(F32), ALU.subtract).then_inc(a.evacuated[ring(y, sl, "Xc")[0]], 1)
                if sl.now:
                    turn(sl, y.rounds - 1)

            over_slots(dve, y, slot)

        def dve_mlp(dve, y):
            m = Ms

            def split_u(g):
                for f in range(FB):
                    dve.wait_ge(m.affined, g * FB + (f + 1))
                    dve.tensor_copy(UT[:, 0, f, :], affine[:, f % 2, :]).then_inc(m.ut_hi, 1)
                    dve.wait_ge(m.ut_hi, g * FB + (f + 1))
                    dve.tensor_tensor(UT[:, 1, f, :], affine[:, f % 2, :], UT[:, 0, f, :].bitcast(F32),
                                      ALU.subtract).then_inc(m.ut_ready, 1)

            def group(g, more):
                for j in range(NBLK):
                    if j >= 4:
                        dve.wait_ge(m.y_step, g * Y_STEPS + (j - 3))
                    elif not isinstance(g, int) or g:
                        done = Y_STEPS if j == 3 else j - 4 + NBLK + 1
                        dve.wait_ge(m.y_step, (g - 1) * Y_STEPS + done)
                    dve.wait_ge(m.gelu_done, g * NBLK + (j + 1))
                    dve.tensor_copy(G[:, j % 4, 0, :], gelu[:, j % 2, :]).then_inc(m.g_hi, 1)
                    dve.wait_ge(m.g_hi, g * NBLK + (j + 1))
                    dve.tensor_tensor(G[:, j % 4, 1, :], gelu[:, j % 2, :], G[:, j % 4, 0, :].bitcast(F32),
                                      ALU.subtract).then_inc(m.g_ready, 1)
                if more:
                    split_u(g + 1)
                dve.wait_ge(m.res_ready, g + 1)
                for r in range(ROWB):
                    dve.wait_ge(m.y_step, g * Y_STEPS + (NBLK + r))
                    dve.tensor_tensor(res[:, r, :], PS[:, r, :], res[:, r, :], ALU.add).then_inc(m.y_added, 1)

            split_u(y.g0)
            group(y.g0, True)
            with dve.Fori(1, GROUPS - 1) as i:
                group(i + y.g0, True)
            group(y.g0 + GROUPS - 1, False)

        def three_passes(pe, dst, lhs, rhs, first, last):
            for n, (i, j) in enumerate(((1, 0), (0, 1), (0, 0))):
                mm = pe.matmul(dst, lhs(i), rhs(j), start=first and n == 0, stop=last and n == 2, skip_group_check=True)
            return mm

        def pe_attention(pe, y):
            a, key = As[y.n], ("a", y.n)
            w = lambda i, f, lo, hi: W[:, y.a0 + i, f * D + lo:f * D + hi]
            n_kv = len(phases[key]) - 8
            if y.n:
                wait_phase_before(pe, y)

            def begin(sl, name):
                k, count, _ = ring(y, sl, name)
                wait(pe, a.evacuated[k], count - 1)
                return bank(y, sl, name)

            def scores(sl, s):
                if s == 0 and sl.ref >= 0:
                    for i in range(y.n_k):
                        wait_evacuated(pe, y, sl, f"K{i}", 1)
                    wait_evacuated(pe, y, sl, "Q", 1)
                free = a.summed if y.kind == GQA else a.exped
                if y.kind != GQA:
                    pe.wait_ge(a.mask_ready, sl.c + 1)
                    if sl.ref == 0 and s == 0:
                        pe.wait_ge(a.zeroed, 2 if y.b0 else 1)
                    for r in range(4):
                        wait(pe, free, step_of(y, sl, s, r) - 4)
                        n = D // y.width
                        pe.matmul(PS[:, r, :].rearrange("p (u n) -> p u n", u=n), first_row[:, :],
                                  mask_row[:, sl.par, 0:y.width].unsqueeze(1).broadcast_to([P, n, y.width]),
                                  start=True, stop=False, skip_group_check=True)
                per = 4 // y.rounds
                for i in range(per):
                    c = per * s + i
                    for r in range(4):
                        if y.kind == GQA and i == 0:
                            wait(pe, free, step_of(y, sl, s, r) - 4)
                        part = slice(32 * r, 32 * r + 32)
                        mm = three_passes(pe, PS[:, r, i * y.width:(i + 1) * y.width],
                                          lambda h: QT[sl.par][part, h, c, :], lambda h: KT[sl.par][part, h, c, 0:y.width],
                                          y.kind == GQA, True)
                        if i == per - 1:
                            mm.then_inc(a.scored, 1)

            def attend(sl, s):
                for r in range(4):
                    dst = begin(sl, f"T{s}_{r}")
                    pe.wait_ge(a.normed, step_of(y, sl, s, r))
                    for t in range(4):
                        mm = pe.transpose(dst[:, t * P:(t + 1) * P], PR[:, r, t * P:(t + 1) * P], ident[:, :])
                    mm.then_inc(a.filled, 1)
                dst = begin(sl, f"O{s}")
                for r in range(4):
                    wait_evacuated(pe, y, sl, f"T{s}_{r}")
                if s == 0:
                    for i in range(y.n_v):
                        wait_evacuated(pe, y, sl, f"V{i}", 1)
                per = 4 // y.rounds
                n_t = 4 // per
                for i in range(per):
                    c = per * s + i
                    for t in range(n_t):
                        for r in range(4):
                            u = 4 * c + r
                            if y.kind == LATENT:
                                v = V[sl.par][:, t, 32 * u:32 * u + 32]
                            elif y.kind == GQA:
                                v = V[sl.par][:, 0, 64 * (u // 2) + 32 * t:64 * (u // 2) + 32 * t + 32]
                            else:
                                v = V[sl.par][:, 0, 32 * u:32 * u + 32]
                            at = (i * n_t + t) * P
                            mm = pe.matmul(dst[32 * r:32 * r + 32, i * P:(i + 1) * P], v, PT[:, r, at:at + P],
                                           start=t == 0, stop=t == n_t - 1, skip_group_check=True)
                mm.then_inc(a.filled, 1)

            def slot(sl):
                if sl.now:
                    scores(sl, 0)
                if sl.nxt:
                    if sl.ref == -1:
                        tiles_ready(pe, key, 3 + n_kv)
                    wait_evacuated(pe, y, sl, "Xx", 1)
                    wait_evacuated(pe, y, sl, "Xc", 1)
                    per = 4 // y.n_k
                    for i in range(y.n_k):
                        dst = begin(sl, f"K{i}")
                        for j in range(per):
                            t = per * i + j
                            for f in range(FB):
                                mm = three_passes(pe, dst[:, j * y.k_cols:(j + 1) * y.k_cols],
                                                  lambda h: w(2 + 2 * h, f, t * P, t * P + P), lambda h: XC[:, h, f, 0:y.k_cols],
                                                  f == 0, f == FB - 1)
                        mm.then_inc(a.filled, 1)
                if sl.prev:
                    if sl.ref == 1:
                        tiles_ready(pe, key, len(phases[key]) - 1)
                    for s in range(y.rounds):
                        wait_evacuated(pe, y, sl, f"O{s}", 1)
                    dst = begin(sl, "out")
                    for f in range(FB):
                        mm = three_passes(pe, dst, lambda h: OT[:, h, f, :], lambda h: w(6 + h, f, 0, D), f == 0, f == FB - 1)
                    mm.then_inc(a.filled, 1)
                if sl.now and y.rounds == 2:
                    attend(sl, 0)
                    scores(sl, 1)
                if sl.nxt:
                    dst = begin(sl, "Q")
                    for t in range(4):
                        for f in range(FB):
                            mm = three_passes(pe, dst[:, t * P:(t + 1) * P], lambda h: w(h, f, t * P, t * P + P),
                                              lambda h: XC[:, h, f, P:2 * P], f == 0, f == FB - 1)
                    mm.then_inc(a.filled, 1)
                    for i in range(y.n_v):
                        dst = begin(sl, f"V{i}")
                        for f in range(FB):
                            if y.kind == GQA:
                                out_, rhs = dst[:, 0:P], (lambda h: W[:, y.a0 + 3 + 2 * h, f * P:(f + 1) * P])
                            else:
                                out_, rhs = dst, (lambda h: w(3 + 2 * h, f, 0, D))
                            mm = three_passes(pe, out_, lambda h: XC[:, h, f, i * P:(i + 1) * P], rhs, f == 0, f == FB - 1)
                        mm.then_inc(a.filled, 1)
                if sl.far:
                    for name, src, loaded in (("Xx", x_nat, a.x_loaded), ("Xc", c_nat, a.c_loaded)):
                        dst = begin(sl, name)
                        pe.wait_ge(loaded, sl.c * 16 + 48)
                        for f in range(FB):
                            mm = pe.transpose(dst[:, f * P:(f + 1) * P], src[:, f * P:(f + 1) * P], ident[:, :])
                        mm.then_inc(a.filled, 1)
                if sl.now:
                    attend(sl, y.rounds - 1)

            over_slots(pe, y, slot)

        def pe_mlp(pe, y):
            m, key = Ms, ("m", y.n)
            pe.wait_ge(As[y.n].unit_ready, y.b0 + B)

            def turn(g):
                pe.wait_ge(m.u_loaded, g * 16 + 16)
                for f in range(FB):
                    wait(pe, m.affined, g * FB + (f - 1))
                    for r in range(ROWB):
                        mm = pe.transpose(PS[:, 6 + f % 2, r * P:(r + 1) * P], u_nat[:, r, f * P:(f + 1) * P], ident[:, :])
                    mm.then_inc(m.turned, 1)

            def up(g, j):
                s = (y.m0 + j) % 16
                if j == 0:
                    pe.wait_ge(m.ut_ready, g * FB + FB)
                tiles_ready(pe, key, 2 * j)
                wait(pe, m.gelu_done, g * NBLK + (j - 1))
                for f in range(FB):
                    mm = three_passes(pe, PS[:, 4 + j % 2, :], lambda h: W[:, s, h * D + f * P:h * D + (f + 1) * P],
                                      lambda h: UT[:, h, f, :], f == 0, f == FB - 1)
                mm.then_inc(m.h_full, 1)

            def down(g, j):
                s = (y.m0 + j) % 16
                tiles_ready(pe, key, 2 * j + 1)
                pe.wait_ge(m.g_ready, g * NBLK + (j + 1))
                for r in range(ROWB):
                    if j == 0:
                        wait(pe, m.y_added, (g - 1) * ROWB + (r + 1))
                    mm = three_passes(pe, PS[:, r, :], lambda h: G[:, j % 4, h, r * P:(r + 1) * P],
                                      lambda h: W[:, s, (2 + h) * D:(3 + h) * D], j == 0, j == NBLK - 1)
                    if j == NBLK - 1 or r == ROWB - 1:
                        mm.then_inc(m.y_step, 1)

            def group(g, more):
                for j in range(NBLK):
                    up(g, j)
                    if j >= 2:
                        down(g, j - 2)
                if more:
                    turn(g + 1)
                down(g, NBLK - 2)
                down(g, NBLK - 1)

            turn(y.g0)
            group(y.g0, True)
            with pe.Fori(1, GROUPS - 1) as i:
                group(i + y.g0, True)
            group(y.g0 + GROUPS - 1, False)

        N_CONSTS = 8
        COLS = []
        for y in L:
            p = f"L{y.n}_xattn_"
            col = lambda name: ins[p + name].rearrange("(t p) -> p t", p=P)
            if y.kind == LATENT:
                kv = ins[p + "kv_b"].rearrange("(t p two) -> p t two", p=P, two=2)
                COLS += [(y.n, 0, 0, col("q_b")), (y.n, 4, 0, kv[:, :, 0]), (y.n, 8, 0, kv[:, :, 1]),
                         (y.n, 12, 0, col("postnorm_w")), (y.n, 28, 0, col("mlp_b1"))]
            elif y.kind == CROSS:
                COLS += [(y.n, 0, 0, col("q_b")), (y.n, 4, 0, col("k_b")), (y.n, 8, 0, col("v_b")), (y.n, 12, 0, col("ln2_w")),
                         (y.n, 16, 0, col("ln2_b")), (y.n, 20, 0, col("ln1_w")), (y.n, 24, 0, col("ln1_b")), (y.n, 28, 0, col("fc_b"))]
            else:
                COLS.append((y.n, 0, 0, col("bq")))
                for e in range(2):
                    for r in range(4):
                        for at, name in ((4, "bk"), (8, "bv")):
                            COLS.append((y.n, at, e * 64 + r * 16, ins[p + name].rearrange("(t e d) -> e d t", e=2, d=16)[e]))

        block = ctx.enter_context(nc.Block())

        @block.sync
        def _(sp):
            for n, at, p0, src in COLS:
                sp.dma_start(cols[p0:p0 + src.shape[0], n, at:at + src.shape[1]], src,
                             allow_slow_non_contiguous=True).then_inc(cols_loaded, 16)
            for i in range(len(phases["a", 0])):
                load_tile(sp, ("a", 0), i)
            sp_attention(sp, L[0])
            sp_mlp(sp, L[0])
            sp_attention(sp, L[1])
            for i in range(len(phases["a", 2])):
                load_tile(sp, ("a", 2), i)
            sp_attention(sp, L[2])
            sp_mlp(sp, L[2])
            sp_attention(sp, L[3])
            sp_mlp(sp, L[3])

        @block.gpsimd
        def _(pool):
            pool.memset(ident[:, :], 0.0).then_inc(ident_zero, 1)
            pool.memset(first_row[:, :], 0.0).then_inc(ident_zero, 1)
            pool.memset(minus_half[:, :], -0.5).then_inc(consts, 1)
            pool.wait_ge(ident_zero, 2)
            pool.memset(first_row[0:1, :], 1.0).then_inc(consts, 1)
            pool.affine_select(out=ident[:, :], in_=ident[:, :], compare_op=ALU.not_equal, fill=1.0, base=0,
                               pattern=[[-1, P]], channel_multiplier=1).then_inc(ident_done, 1)
            pool.wait_ge(consts, N_CONSTS)
            for i in range(len(phases["a", 0])):
                split_tile(pool, ("a", 0), i)
            pool_attention(pool, L[0])
            pool_mlp(pool, L[0])
            pool_attention(pool, L[1])
            for i in range(len(phases["a", 2])):
                split_tile(pool, ("a", 2), i)
            pool_attention(pool, L[2])
            pool_mlp(pool, L[2])
            pool_attention(pool, L[3])
            pool_mlp(pool, L[3])

        @block.vector
        def _(dve):
            dve.wait_ge(cols_loaded, 16 * len(COLS))
            for y in L:
                dve.tensor_scalar(cols[:, y.n, 0:4], cols[:, y.n, 0:4], y.scale, None, ALU.mult).then_inc(consts, 1)
            dve.wait_ge(ident_done, 1)
            groups = ident[:, :].rearrange("p (g two d) -> p g two d", two=2, d=16)
            dve.tensor_reduce(even[:, :], groups[:, :, 0, :], AX.XY, ALU.add).then_inc(consts, 1)
            dve.tensor_reduce(odd[:, :], groups[:, :, 1, :], AX.XY, ALU.add).then_inc(consts, 1)
            dve_attention(dve, L[0])
            dve_mlp(dve, L[0])
            dve_attention(dve, L[1])
            dve_attention(dve, L[2])
            dve_mlp(dve, L[2])
            dve_attention(dve, L[3])
            dve_mlp(dve, L[3])

        @block.scalar
        def _(act):
            act_attention(act, L[0])
            act_mlp(act, L[0])
            act_attention(act, L[1])
            act_attention(act, L[2])
            act_mlp(act, L[2])
            act_attention(act, L[3])
            act_mlp(act, L[3])

        @block.tensor
        def _(pe):
            pe.wait_ge(consts, N_CONSTS)
            pe_attention(pe, L[0])
            pe_mlp(pe, L[0])
            pe_attention(pe, L[1])
            pe_attention(pe, L[2])
            pe_mlp(pe, L[2])
            pe_attention(pe, L[3])
            pe_mlp(pe, L[3])


def kernel(**inputs):
    import concourse.bacc as _bacc
    from concourse.bass_utils import run_bass_kernel_spmd as _run

    nc = _bacc.Bacc("TRN2", target_bir_lowering=False, num_devices=1)
    arrays, ins = {}, {}
    for name, value in inputs.items():
        a = np.ascontiguousarray(value)
        if a.dtype == np.bool_:
            a = a.view(np.uint8)
        arrays[name] = a
        ins[name] = nc.dram_tensor(name, a.shape, mybir.dt.from_np(a.dtype), kind="ExternalInput").ap()
    out = nc.dram_tensor("out", (B, P, D), F32, kind="ExternalOutput").ap()
    build(nc, ins, out)
    r = _run(nc, [arrays], core_ids=[0])
    return r.results[0]["out"]
```
